# Optimizing a Trainium2 kernel written in Bass

```python
import numpy as np
import jax
import jax.numpy as jnp

def _softmax(x, axis=-1):
    return jax.nn.softmax(x, axis=axis)
def _gelu(x):
    return jax.nn.gelu(x, approximate=True)
def _silu(x):
    return jax.nn.silu(x)
def _sigmoid(x):
    return jax.nn.sigmoid(x)
def _layernorm(x, axis=-1, eps=1e-5):
    m = jnp.mean(x, axis=axis, keepdims=True)
    v = jnp.var(x, axis=axis, keepdims=True)
    return (x - m) / jnp.sqrt(v + eps)
def _scatter_add(tgt, idx, src, axis=0):
    return tgt.at[idx].add(src)
def _segment_sum(src, seg, n):
    return jax.ops.segment_sum(src, seg, n)

kernel_name = 'mk_metaformer_d1_conv_nhwc256_391ef7'

def setup_inputs(seed: int = 0):
    np.random.seed(seed)
    _w = jnp.asarray
    def _rec_inputs():
        import jax
        import jax.numpy as jnp
        _gk = jax.random.key(seed)
        x = -6.817e-05 + 0.9999 * jax.random.normal(jax.random.fold_in(_gk, 1), (4, 64, 64, 256), jnp.float32)
        return x
    x = _rec_inputs()
    def _L0_conv_setup():
        import jax, jax.numpy as jnp
        import numpy as np
        NB_POOLS = 256
        key = jax.random.key(seed)
        x = jax.random.normal(key, (4, 64, 64, 256), dtype=jnp.float32)
        return {'x': x}
    _L0_conv_all = _L0_conv_setup()
    _L0_conv_in = {k: v for k, v in _L0_conv_all.items() if k in ()}
    del _L0_conv_all

    def _L0_ffn_setup():
        import jax, jax.numpy as jnp
        import numpy as np
        B, N, D = (16, 4096, 256)
        NUM_EXPERTS, TOP_K, HEADS = (4, 2, 4)
        N_EDGES = 1048576
        LN_EPS = 1e-05

        def _layernorm(x, g, b):
            mu = x.mean(-1, keepdims=True)
            var = ((x - mu) ** 2).mean(-1, keepdims=True)
            return (x - mu) * jax.lax.rsqrt(var + LN_EPS) * g + b

        def _forward(x, edge_index, W_gat, att_src, att_dst, b_gat, ln_gamma, ln_beta, W1, b1, W2, b2):
            Bc, Nc, Dc = x.shape
            M = Bc * Nc
            x_flat = x.reshape(M, Dc)
            h = (x_flat @ W_gat).reshape(M, HEADS, NUM_EXPERTS)
            loops = jnp.arange(M, dtype=edge_index.dtype)
            src = jnp.concatenate([edge_index[0], loops])
            dst = jnp.concatenate([edge_index[1], loops])
            a_src = (h * att_src).sum(-1)
            a_dst = (h * att_dst).sum(-1)
            e = jax.nn.leaky_relu(a_src[src] + a_dst[dst], negative_slope=0.2)
            e_max = jax.ops.segment_max(e, dst, num_segments=M)
            ee = jnp.exp(e - e_max[dst])
            denom = jax.ops.segment_sum(ee, dst, num_segments=M)
            alpha = ee / (denom[dst] + 1e-16)
            msg = h[src] * alpha[:, :, None]
            agg = jax.ops.segment_sum(msg, dst, num_segments=M).reshape(M, HEADS * NUM_EXPERTS) + b_gat
            scores = _layernorm(agg, ln_gamma, ln_beta).reshape(M, HEADS, NUM_EXPERTS).mean(1)
            scores = scores.reshape(Bc, Nc, NUM_EXPERTS)
            topk_s, topk_i = jax.lax.top_k(scores, TOP_K)
            w = jax.nn.softmax(topk_s, axis=-1)
            out = jnp.zeros_like(x)
            for ei in range(NUM_EXPERTS):
                g = jnp.where(topk_i == ei, w, 0.0).sum(-1)
                hh = jax.nn.gelu(x @ W1[ei] + b1[ei], approximate=False)
                out = out + g[..., None] * (hh @ W2[ei] + b2[ei])
            return out
        key = jax.random.key(seed)
        ks = jax.random.split(key, 8)
        s = 0.05
        return {'x': jax.random.normal(ks[0], (B, N, D), jnp.float32), 'W_gat': jax.random.normal(ks[1], (D, HEADS * NUM_EXPERTS), jnp.float32) * s, 'att_src': jax.random.normal(ks[2], (HEADS, NUM_EXPERTS), jnp.float32) * s, 'att_dst': jax.random.normal(ks[3], (HEADS, NUM_EXPERTS), jnp.float32) * s, 'b_gat': jnp.zeros((HEADS * NUM_EXPERTS,), jnp.float32), 'ln_gamma': jnp.ones((HEADS * NUM_EXPERTS,), jnp.float32), 'ln_beta': jnp.zeros((HEADS * NUM_EXPERTS,), jnp.float32), 'W1': jax.random.normal(ks[4], (NUM_EXPERTS, D, 2 * D), jnp.float32) * s, 'b1': jnp.zeros((NUM_EXPERTS, 2 * D), jnp.float32), 'W2': jax.random.normal(ks[5], (NUM_EXPERTS, 2 * D, D), jnp.float32) * s, 'b2': jnp.zeros((NUM_EXPERTS, D), jnp.float32), 'edge_index': jax.random.randint(ks[6], (2, N_EDGES), 0, B * N, jnp.int32)}
    _L0_ffn_all = _L0_ffn_setup()
    _L0_ffn_in = {k: v for k, v in _L0_ffn_all.items() if k in ('W_gat', 'att_src', 'att_dst', 'b_gat', 'ln_gamma', 'ln_beta', 'W1', 'b1', 'W2', 'b2', 'edge_index', )}
    del _L0_ffn_all

    return {
        "x": x,
        "L0_ffn_W_gat": _L0_ffn_in["W_gat"],
        "L0_ffn_att_src": _L0_ffn_in["att_src"],
        "L0_ffn_att_dst": _L0_ffn_in["att_dst"],
        "L0_ffn_b_gat": _L0_ffn_in["b_gat"],
        "L0_ffn_ln_gamma": _L0_ffn_in["ln_gamma"],
        "L0_ffn_ln_beta": _L0_ffn_in["ln_beta"],
        "L0_ffn_W1": _L0_ffn_in["W1"],
        "L0_ffn_b1": _L0_ffn_in["b1"],
        "L0_ffn_W2": _L0_ffn_in["W2"],
        "L0_ffn_b2": _L0_ffn_in["b2"],
        "L0_ffn_edge_index": _L0_ffn_in["edge_index"],
    }

def reference(x, L0_ffn_W_gat, L0_ffn_att_src, L0_ffn_att_dst, L0_ffn_b_gat, L0_ffn_ln_gamma, L0_ffn_ln_beta, L0_ffn_W1, L0_ffn_b1, L0_ffn_W2, L0_ffn_b2, L0_ffn_edge_index):
    import jax
    import jax.numpy as jnp
    def _L0_conv_ref(x):
        import jax, jax.numpy as jnp
        import numpy as np
        NB_POOLS = 256
        B, H, W, F = x.shape
        M = H * W
        x3 = x.reshape(B, M, F)
        corr = jnp.einsum('bmf,bnf->bmn', x3, x3) / F
        s = -jnp.sort(-corr, axis=-1)
        ranks = jnp.round(jnp.linspace(1.0, M - 1, NB_POOLS)).astype(jnp.int32)
        pooled = jnp.take(s, ranks, axis=-1)
        return pooled.reshape(B, H, W, NB_POOLS)

    def _L0_ffn_ref(x, W_gat, att_src, att_dst, b_gat, ln_gamma, ln_beta, W1, b1, W2, b2, edge_index):
        import jax, jax.numpy as jnp
        import numpy as np
        B, N, D = (16, 4096, 256)
        NUM_EXPERTS, TOP_K, HEADS = (4, 2, 4)
        N_EDGES = 1048576
        LN_EPS = 1e-05

        def _layernorm(x, g, b):
            mu = x.mean(-1, keepdims=True)
            var = ((x - mu) ** 2).mean(-1, keepdims=True)
            return (x - mu) * jax.lax.rsqrt(var + LN_EPS) * g + b

        def _forward(x, edge_index, W_gat, att_src, att_dst, b_gat, ln_gamma, ln_beta, W1, b1, W2, b2):
            Bc, Nc, Dc = x.shape
            M = Bc * Nc
            x_flat = x.reshape(M, Dc)
            h = (x_flat @ W_gat).reshape(M, HEADS, NUM_EXPERTS)
            loops = jnp.arange(M, dtype=edge_index.dtype)
            src = jnp.concatenate([edge_index[0], loops])
            dst = jnp.concatenate([edge_index[1], loops])
            a_src = (h * att_src).sum(-1)
            a_dst = (h * att_dst).sum(-1)
            e = jax.nn.leaky_relu(a_src[src] + a_dst[dst], negative_slope=0.2)
            e_max = jax.ops.segment_max(e, dst, num_segments=M)
            ee = jnp.exp(e - e_max[dst])
            denom = jax.ops.segment_sum(ee, dst, num_segments=M)
            alpha = ee / (denom[dst] + 1e-16)
            msg = h[src] * alpha[:, :, None]
            agg = jax.ops.segment_sum(msg, dst, num_segments=M).reshape(M, HEADS * NUM_EXPERTS) + b_gat
            scores = _layernorm(agg, ln_gamma, ln_beta).reshape(M, HEADS, NUM_EXPERTS).mean(1)
            scores = scores.reshape(Bc, Nc, NUM_EXPERTS)
            topk_s, topk_i = jax.lax.top_k(scores, TOP_K)
            w = jax.nn.softmax(topk_s, axis=-1)
            out = jnp.zeros_like(x)
            for ei in range(NUM_EXPERTS):
                g = jnp.where(topk_i == ei, w, 0.0).sum(-1)
                hh = jax.nn.gelu(x @ W1[ei] + b1[ei], approximate=False)
                out = out + g[..., None] * (hh @ W2[ei] + b2[ei])
            return out
        return _forward(x, edge_index, W_gat, att_src, att_dst, b_gat, ln_gamma, ln_beta, W1, b1, W2, b2)

    def _gn(v, G=32, eps=1e-5):
        B_, H_, W_, C_ = v.shape
        g = v.reshape(B_, H_, W_, G, C_ // G)
        m = jnp.mean(g, axis=(1, 2, 4), keepdims=True)
        s = jnp.var(g, axis=(1, 2, 4), keepdims=True)
        return ((g - m) / jnp.sqrt(s + eps)).reshape(v.shape)

    def _ln_c(v, eps=1e-6):
        m = jnp.mean(v, axis=-1, keepdims=True)
        s = jnp.var(v, axis=-1, keepdims=True)
        return (v - m) / jnp.sqrt(s + eps)

    def _ln_t(v, eps=1e-5):
        m = jnp.mean(v, axis=-1, keepdims=True)
        s = jnp.var(v, axis=-1, keepdims=True)
        return (v - m) / jnp.sqrt(s + eps)

    def _to_tokens(v):
        B_, H_, W_, C_ = v.shape
        return v.reshape(B_, H_ * W_, C_)
    def _from_tokens(t, like):
        return t.reshape(like.shape)

    x = x + _L0_conv_ref(_ln_c(x))
    t = _to_tokens(x)
    t = t + _L0_ffn_ref(_ln_t(t), L0_ffn_W_gat, L0_ffn_att_src, L0_ffn_att_dst, L0_ffn_b_gat, L0_ffn_ln_gamma, L0_ffn_ln_beta, L0_ffn_W1, L0_ffn_b1, L0_ffn_W2, L0_ffn_b2, L0_ffn_edge_index)
    x = _from_tokens(t, x)
    return x


_drawn_inputs = setup_inputs


def setup_inputs(seed=0):
    import zlib

    import numpy as np

    out = dict(_drawn_inputs(seed))
    spreads = {'L0_ffn_b_gat': (0.0, 0.1),
     'L0_ffn_ln_gamma': (1.0, 0.2),
     'L0_ffn_ln_beta': (0.0, 0.1),
     'L0_ffn_b1': (0.0, 0.1),
     'L0_ffn_b2': (0.0, 0.1)}
    factors = {}
    for name, (base, spread) in spreads.items():
        noise = np.random.default_rng([zlib.crc32(name.encode()), seed]).standard_normal(out[name].shape)
        drawn = base * np.exp(spread * noise) if base else spread * noise
        out[name] = jnp.asarray(drawn.astype(out[name].dtype))
    for name, factor in factors.items():
        out[name] = (out[name] * factor).astype(out[name].dtype)
    return out
```

```python
import numpy as np
import concourse.bass as bass
from concourse import mybir

F32 = mybir.dt.float32
BF16 = mybir.dt.bfloat16
I32 = mybir.dt.int32
ALU = mybir.AluOpType
ACT = mybir.ActivationFunctionType
AX = mybir.AxisListType

P = 128
IMAGES, SIDE, D = 4, 64, 256
M = SIDE * SIDE
TOKENS = IMAGES * M
TILES = TOKENS // P
PAIRS = TILES // 2
PAIRS_OF_IMAGE = M // P // 2
DC = D // P
BANK = 512
CORR_CHUNKS = M // BANK

EXPERTS, HEADS, HID = 4, 4, 512
HC = HID // P
GAT = HEADS * EXPERTS
TAB = HEADS + GAT + HEADS
LN_C_EPS, LN_T_EPS, LN_G_EPS = 1e-6, 1e-5, 1e-5

EDGES = 1048576
ECOLS = EDGES // P
ECHUNK = 512
EQ = 4
CHUNK = EQ * P
MAX_CHUNKS = EDGES // CHUNK + TILES
CHUNK_COLS = (MAX_CHUNKS + 8 + P - 1) // P
MOST_PAIRS = (MAX_CHUNKS + 3) // 4 * 2
CAPACITY = CHUNK_COLS * P * CHUNK
SENTINEL = 255
BIG = float(2 ** 21)
MASKED = -1.0e30
SUPER = P
GROUPS = SUPER // 4
SCAT = 128
SCAT_SEMS = 8
SUM_SLOTS = 4

C_IDENT, C_RANK, C_ONES, C_IOTA = 0, P, 2 * P, 3 * P
C_DIAG = 4 * P
C_FOLD = C_DIAG + 64
C_CID = C_FOLD + 16
C_WINDOW = C_CID + CHUNK_COLS
C_BEFORE = C_WINDOW + 2 * P - 1
C_PICK = C_BEFORE + 3 * GROUPS
C_ALL = C_PICK + GROUPS


def shape_constants():
    c = np.zeros((P, C_ALL), np.float32)
    r = np.arange(P)
    c[:, C_IDENT:C_IDENT + P] = np.eye(P)
    c[:, C_RANK:C_RANK + P] = (r[:, None] < r[None, :]) + BIG * np.eye(P)
    c[:, C_ONES:C_ONES + P] = 1.0
    c[:, C_IOTA:C_IOTA + P] = r[None, :]
    c[:, C_DIAG:C_DIAG + 64] = (r[:, None] // 16) == (np.arange(64)[None, :] // 8)
    c[:, C_FOLD:C_FOLD + 16] = (r[:, None] % 16) == np.arange(16)[None, :]
    c[:, C_WINDOW + P - 1] = 1.0
    c[:, C_BEFORE:C_BEFORE + 3 * GROUPS] = r[:, None] < 4 * (np.arange(3 * GROUPS) % GROUPS)[None, :]
    g = r[:3 * GROUPS]
    c[:3 * GROUPS, C_PICK:C_PICK + GROUPS] = (256.0 ** (g // GROUPS))[:, None] * (
        (g % GROUPS)[:, None] == np.arange(GROUPS)[None, :])
    c[:, C_CID:C_CID + CHUNK_COLS] = r[:, None] + P * np.arange(CHUNK_COLS)[None, :]
    return c


def sort_stages():
    out, p = [], 1
    while p < M:
        k = p
        while k >= 1:
            out.append((p, k))
            k //= 2
        p *= 2
    return out


STAGES = sort_stages()
N_STAGES = len(STAGES)
N_CARRIED = sum(k < p for p, k in STAGES)


def compared(buf, p, k):
    v = buf.rearrange("p (n b) -> p n b", b=2 * p)
    if k == p:
        return v[:, :, 0:p], v[:, :, p:2 * p], []
    m = v[:, :, k:2 * p - k].rearrange("p n (g two i) -> p n g two i", two=2, i=k)
    return m[:, :, :, 0, :], m[:, :, :, 1, :], [v[:, :, 0:k], v[:, :, 2 * p - k:2 * p]]


def rank_runs():
    ranks = [int(r) for r in np.round(np.linspace(1.0, M - 1, D))]
    runs, i = [], 0
    while i < D:
        n = 1
        while i + n < D and ranks[i + n] - ranks[i + n - 1] == 16:
            n += 1
        runs.append((i, ranks[i], n))
        i += n
    return runs


RUNS = rank_runs()


class Tally:

    def __init__(self, engine, sem, base=0):
        self.engine, self.sem, self.base, self.n = engine, sem, base, 0

    def mark(self, instruction):
        self.n += 1
        return instruction.then_inc(self.sem, 1)

    def wait(self):
        self.engine.wait_ge(self.sem, self.base + self.n)

    def then(self, instruction):
        self.mark(instruction)
        self.wait()


class Buffers:
    pass


def build(nc, x, w_gat, att_src, att_dst, b_gat, ln_gamma, ln_beta, w1, b1, w2, b2, edges, consts, out):
    sb = nc.alloc_sbuf_tensor
    sem = nc.alloc_semaphore

    def scratch(name, shape, dt=F32):
        return nc.dram_tensor(name, shape, dt, kind="Internal").ap()

    settled = [sem(f"settled_{e}") for e in ("vector", "gpsimd", "sync")]

    xnt_d = scratch("xnt_d", [P, DC, TOKENS])
    x2_d = scratch("x2_d", [TILES, P, D])
    y_d = scratch("y_d", [TILES, P, EXPERTS * D])
    table_d = scratch("table_d", [TOKENS, TAB])
    words_d = scratch("words_d", [P, ECOLS], I32)
    place_d = scratch("place_d", [P, ECOLS], I32)
    sorted_d = scratch("sorted_d", [CAPACITY, 1], I32)
    chunk_tile_d = scratch("chunk_tile_d", [CHUNK_COLS, P], I32)
    loops_d = scratch("loops_d", [1, 2], I32)
    gathered_d = scratch("gathered_d", [CHUNK_COLS * P, P, EQ * TAB])

    x_t = x.rearrange("b h w d -> (b h w) d").rearrange("(t p) d -> t p d", p=P)
    out_t = out.rearrange("b h w d -> (b h w) d").rearrange("(t p) d -> t p d", p=P)

    arena = sb("arena", [P, 6 * M], F32)
    xnt = sb("xnt", [P, DC, M], F32)
    w1s = sb("w1s", [P, EXPERTS, DC, HID], F32)
    w2s = sb("w2s", [P, EXPERTS, HC, D], F32)
    b1s = sb("b1s", [P, EXPERTS, HC], F32)
    b2s = sb("b2s", [1, EXPERTS * D], F32)
    wtab = sb("wtab", [P, DC, TAB], F32)
    cst = sb("cst", [P, C_ALL], F32)
    gat = sb("gat", [P, 5, GAT], F32)
    rank_bf = sb("rank_bf", [P, P], BF16)
    ones_bf = sb("ones_bf", [P, P], BF16)
    iota_bf = sb("iota_bf", [P, P], BF16)
    order_bf = sb("order_bf", [P, C_ALL - C_WINDOW], BF16)
    eps = sb("eps", [P, 3], F32)
    counts = sb("counts", [P, 64], F32)
    psum = nc.alloc_psum_tensor("psum", [P, 8, BANK], F32)

    ident = cst[:, C_IDENT:C_IDENT + P]
    ones = cst[:, C_ONES:C_ONES + P]
    iota = cst[:, C_IOTA:C_IOTA + P]

    def carve(first, shape, dt=F32):
        n = int(np.prod(shape))
        width = n if dt in (F32, I32) else n // 2
        v = arena[:, first:first + width]
        if dt is not F32:
            v = v.bitcast(dt)
        if len(shape) == 2:
            return v.rearrange("p (a b) -> p a b", a=shape[0])
        if len(shape) == 3:
            return v.rearrange("p (a b c) -> p a b c", a=shape[0], b=shape[1])
        return v

    b = Buffers()
    b.arena, b.att_dst, b.att_src, b.b1, b.b1s, b.b2 = (
        arena, att_dst, att_src, b1, b1s, b2)
    b.b2s, b.b_gat, b.carve, b.chunk_tile_d, b.consts, b.counts = (
        b2s, b_gat, carve, chunk_tile_d, consts, counts)
    b.cst, b.edges, b.eps, b.gat, b.gathered_d, b.ident = (
        cst, edges, eps, gat, gathered_d, ident)
    b.iota, b.iota_bf, b.ln_beta, b.ln_gamma, b.loops_d, b.ones = (
        iota, iota_bf, ln_beta, ln_gamma, loops_d, ones)
    b.ones_bf, b.order_bf, b.out_t, b.place_d, b.psum, b.rank_bf = (
        ones_bf, order_bf, out_t, place_d, psum, rank_bf)
    b.sb, b.sem, b.settled, b.sorted_d, b.table_d, b.w1 = (
        sb, sem, settled, sorted_d, table_d, w1)
    b.w1s, b.w2, b.w2s, b.w_gat, b.words_d, b.wtab = (
        w1s, w2, w2s, w_gat, words_d, wtab)
    b.x2_d, b.x_t, b.xnt, b.xnt_d, b.y_d = (
        x2_d, x_t, xnt, xnt_d, y_d)
    prepare(nc, b)
    rank(nc, b)
    pool_rows(nc, b)
    segment_max(nc, b)
    segment_sum(nc, b)
    route(nc, b)
    combine(nc, b)


def prepare(nc, b):
    sem, carve, psum = b.sem, b.carve, b.psum
    const_in, weight_in = sem("const_in"), sem("weight_in")
    consts_cast = sem("consts_cast")
    edge_in = [sem(f"edge_in{s}") for s in range(2)]
    word_out = [sem(f"word_out{s}") for s in range(2)]
    words_made, edges_read = sem("words_made"), sem("edges_read")
    hot_ready, hot_used = sem("hot_ready"), sem("hot_used")
    fill_ready, fill_out = sem("fill_ready"), sem("fill_out")
    x_in = [sem(f"x_in{s}") for s in range(2)]
    xt_out = [sem(f"xt_out{s}") for s in range(2)]
    stats_ready, std_ready, normed, turned, turned_copied = (
        sem("stats_ready"), sem("std_ready"), sem("normed"), sem("turned"), sem("turned_copied"))
    dve_step = sem("dve_step_prepare")

    hi_all = carve(0, [ECOLS + SUPER], BF16)
    at = (ECOLS + SUPER) // 2
    src_in = carve(at, [2, ECHUNK], I32)
    dst_in = carve(at + 1024, [2, ECHUNK], I32)
    words = carve(at + 2048, [2, ECHUNK], I32)
    hi4 = carve(at + 3072, [ECHUNK], I32)
    lo3 = carve(at + 3584, [ECHUNK], I32)
    lo7 = carve(at + 4096, [ECHUNK], I32)
    hi = carve(at + 4608, [ECHUNK], I32)
    hot16 = [carve(at + 5120 + 512 * s, [64, 16], BF16) for s in range(2)]
    hot8 = [carve(at + 6144 + 256 * s, [64, 8], BF16) for s in range(2)]
    xs = [carve(at + 6656 + 1024 * s, [4, D]) for s in range(2)]
    xn = [carve(at + 8704 + 1024 * s, [4, D]) for s in range(2)]
    xt = [b.xnt[:, :, s * 512:s * 512 + 512] for s in range(2)]
    stat = carve(at + 10752, [4, 6])
    mv = carve(at + 10776, [2, 4, 2])
    std = carve(at + 10792, [2, 4])
    rstd = carve(at + 10800, [4])
    var = carve(at + 10804, [4])
    rtmp = carve(at + 10808, [4])
    fill = carve(at + 10816, [CAPACITY // P // 4], I32)
    tmp = b.sb("tmp_wtab", [P, GAT], F32)

    edges_v = b.edges.rearrange("s (p j) -> s p j", p=P)
    x_q = b.x_t.rearrange("(g q) p d -> g p q d", q=4)
    N_E = ECOLS // ECHUNK // 2
    SUBS = ECHUNK // 64
    N_X = TILES // 8

    with nc.Block() as block:
        @block.sync
        def _(sp):
            sp.dma_start(b.cst[:], b.consts[:, :]).then_inc(const_in, 16)
            for n, v in enumerate((b.att_src.rearrange("h e -> (h e)"), b.att_dst.rearrange("h e -> (h e)"), b.b_gat,
                                   b.ln_gamma, b.ln_beta)):
                sp.dma_start(b.gat[:, n, :], v.rearrange("(o k) -> o k", o=1).broadcast_to([P, GAT])).then_inc(
                    const_in, 16)
            sp.dma_start(b.wtab[:, :, HEADS:HEADS + GAT], b.w_gat.rearrange("(c p) n -> p c n", p=P)).then_inc(
                const_in, 16)
            with sp.Fori(0, N_E) as i:
                for s in range(2):
                    sp.wait_ge(edges_read, (i * 2 + s) if s == 0 else i * 2)
                    col = (i * 2 + s) * ECHUNK
                    sp.dma_start(src_in[:, s, :], edges_v[0, :, bass.ds(col, ECHUNK)]).then_inc(edge_in[s], 16)
                    sp.dma_start(dst_in[:, s, :], edges_v[1, :, bass.ds(col, ECHUNK)]).then_inc(edge_in[s], 16)
            for e in range(EXPERTS):
                sp.dma_start(b.w1s[:, e], b.w1[e].rearrange("(c p) f -> p c f", p=P)).then_inc(weight_in, 16)
                sp.dma_start(b.w2s[:, e], b.w2[e].rearrange("(m p) f -> p m f", p=P)).then_inc(weight_in, 16)
                with nc.allow_non_contiguous_dma("biases by hidden unit"):
                    sp.dma_start(b.b1s[:, e, :], b.b1[e].rearrange("(m p) -> p m", p=P)).then_inc(weight_in, 16)
            sp.dma_start(b.b2s[:], b.b2.rearrange("e d -> (e d)").rearrange("(o k) -> o k", o=1)).then_inc(
                weight_in, 16)
            for s in range(2):
                sp.dma_start(xs[s], x_q[s]).then_inc(x_in[s], 16)
            with sp.Fori(0, N_X) as i:
                for s in range(2):
                    sp.wait_ge(turned_copied, i * 2 + s + 1)
                    tok = (i * 2 + s) * 512
                    sp.dma_start(b.xnt_d[:, :, bass.ds(tok, 512)], xt[s]).then_inc(xt_out[s], 16)
                    nxt = ((i * 2 + s + 2) % (TILES // 4))
                    sp.dma_start(xs[s], x_q[bass.ds(nxt, 1)].rearrange("o p q d -> (o p) q d")).then_inc(x_in[s], 16)
            sp.wait_ge(fill_out, 64)
            sp.wait_ge(weight_in, 16 * (3 * EXPERTS + 1))
            for s in range(2):
                sp.wait_ge(xt_out[s], 16 * N_X)
                sp.wait_ge(word_out[s], 16 * N_E)
                sp.wait_ge(x_in[s], 16 * (N_X + 1))

        @block.vector
        def _(dve):
            t = Tally(dve, dve_step)
            nc.vector.memset(b.eps[:, 0:1], LN_C_EPS)
            nc.vector.memset(b.eps[:, 1:2], LN_T_EPS)
            nc.vector.memset(b.eps[:, 2:3], LN_G_EPS)
            nc.vector.memset(fill, SENTINEL).then_inc(fill_ready, 1)
            nc.vector.memset(b.counts[:], 0.0)
            nc.vector.memset(hi_all[:, ECOLS:], 200.0)
            dve.wait_ge(const_in, 16 * 7)
            nc.vector.tensor_copy(b.rank_bf[:], b.cst[:, C_RANK:C_RANK + P])
            nc.vector.tensor_copy(b.ones_bf[:], b.ones)
            nc.vector.tensor_copy(b.order_bf[:], b.cst[:, C_WINDOW:C_ALL])
            nc.vector.tensor_copy(b.iota_bf[:], b.iota).then_inc(consts_cast, 1)
            for c in range(DC):
                for n, at_ in ((0, 0), (1, HEADS + GAT)):
                    t.then(nc.vector.tensor_tensor(tmp[:], b.wtab[:, c, HEADS:HEADS + GAT], b.gat[:, n, :], ALU.mult))
                    t.then(nc.vector.tensor_reduce(b.wtab[:, c, at_:at_ + HEADS],
                                                   tmp[:].rearrange("p (h e) -> p h e", h=HEADS), AX.X, ALU.add))
            base = t.n
            STEPS = 1
            with dve.Fori(0, N_E) as i:
                for s in range(2):
                    k = i * 2 + s
                    t = Tally(dve, dve_step, base=k * STEPS + base)
                    dve.wait_ge(edge_in[s], (i + 1) * 32)
                    dve.wait_ge(word_out[s], i * 16)
                    dst, src = dst_in[:, s, :], src_in[:, s, :]
                    nc.vector.tensor_scalar(hi4, dst, 10, None, ALU.logical_shift_right)
                    nc.vector.tensor_scalar(lo3, dst, 7, 7, ALU.logical_shift_right, ALU.bitwise_and)
                    nc.vector.tensor_scalar(hi, dst, 7, None, ALU.logical_shift_right)
                    nc.vector.tensor_scalar(lo7, dst, P - 1, None, ALU.bitwise_and)
                    t.then(nc.vector.tensor_scalar(words[:, s, :], src, float(TOKENS - 1), 256.0, ALU.min, ALU.mult))
                    nc.vector.tensor_scalar(hi_all[:, bass.ds(k * ECHUNK, ECHUNK)], hi, 200.0, None, ALU.min)
                    nc.vector.tensor_tensor(words[:, s, :], words[:, s, :], lo7, ALU.bitwise_or).then_inc(words_made, 1)
                    for u in range(SUBS):
                        h = u % 2
                        dve.wait_ge(hot_used, k * SUBS + max(u - 1, 0))
                        cols = slice(u * 64, u * 64 + 64)
                        nc.vector.tensor_tensor(hot16[h], hi4[:, cols].unsqueeze(2).broadcast_to([P, 64, 16]),
                                                b.iota[:, 0:16].unsqueeze(1).broadcast_to([P, 64, 16]), ALU.is_equal)
                        nc.vector.tensor_tensor(hot8[h], lo3[:, cols].unsqueeze(2).broadcast_to([P, 64, 8]),
                                                     b.iota[:, 0:8].unsqueeze(1).broadcast_to([P, 64, 8]),
                                                     ALU.is_equal).then_inc(hot_ready, 1)
                    dve.wait_ge(hot_used, (k + 1) * SUBS)
                    dve.wait_ge(edges_read, k)
                    nc.vector.tensor_tensor(b.counts[:], b.counts[:], psum[:, 0, 0:64], ALU.add).then_inc(
                        edges_read, 1)
            x_base = base + 2 * N_E * STEPS
            X_STEPS = 7
            with dve.Fori(0, N_X) as i:
                for s in range(2):
                    k = i * 2 + s
                    t = Tally(dve, dve_step, base=k * X_STEPS + x_base)
                    dve.wait_ge(x_in[s], (i + 1) * 16)
                    for q in range(4):
                        last = nc.vector.bn_stats(stat[:, q, :], xs[s][:, q, :])
                    t.then(last)
                    dve.sem_inc(b.settled[0], 1)
                    for q in range(4):
                        last = nc.vector.bn_aggr(mv[:, s, q, :], stat[:, q, :])
                    t.then(last)
                    nc.vector.tensor_scalar(var, mv[:, s, :, 1], LN_C_EPS, None, ALU.add).then_inc(stats_ready, 1)
                    dve.wait_ge(std_ready, k + 1)
                    newton(nc, t, rstd, rtmp, var, std[:, s, :])
                    dve.wait_ge(turned, k)
                    for q in range(4):
                        last = nc.vector.tensor_scalar(xn[s][:, q, :], xs[s][:, q, :], mv[:, s, q, 0:1],
                                                       rstd[:, q:q + 1], ALU.subtract, ALU.mult)
                    last.then_inc(normed, 1)

        @block.tensor
        def _(pe):
            pe.wait_ge(consts_cast, 1)
            with pe.Fori(0, 2 * N_E) as k:
                pe.wait_ge(edges_read, k)
                for u in range(SUBS):
                    pe.wait_ge(hot_ready, k * SUBS + u + 1)
                    l16 = hot16[u % 2].rearrange("p j b -> p (j b)")
                    l8 = hot8[u % 2].rearrange("p j b -> p (j b)")
                    for g in range(8):
                        last = nc.tensor.matmul(psum[:, 0, 0:64], l16[:, g * 128:g * 128 + 128],
                                                l8[:, g * 64:g * 64 + 64], start=(u == 0 and g == 0),
                                                stop=(u == SUBS - 1 and g == 7))
                    last.then_inc(hot_used, 1)
            with pe.Fori(0, N_X) as i:
                for s in range(2):
                    k = i * 2 + s
                    pe.wait_ge(normed, k + 1)
                    pe.wait_ge(turned_copied, k)
                    for c in range(DC):
                        for q in range(4):
                            last = nc.tensor.transpose(psum[:, 1 + 2 * s + c, q * P:q * P + P],
                                                       xn[s][:, q, c * P:c * P + P], b.ident)
                    last.then_inc(turned, 1)

        @block.scalar
        def _(act):
            act.wait_ge(fill_ready, 1)
            fr = b.sorted_d.rearrange("(a p k) o -> a p (k o)", a=4, p=P)
            for a in range(4):
                act.dma_start(fr[a], fill).then_inc(fill_out, 16)
            with act.Fori(0, N_E) as i:
                for s in range(2):
                    k = i * 2 + s
                    act.wait_ge(words_made, k + 1)
                    act.dma_start(b.words_d[:, bass.ds(k * ECHUNK, ECHUNK)], words[:, s, :]).then_inc(word_out[s], 16)
            with act.Fori(0, N_X) as i:
                for s in range(2):
                    k = i * 2 + s
                    act.wait_ge(stats_ready, k + 1)
                    nc.scalar.activation(std[:, s, :], var, ACT.Sqrt).then_inc(std_ready, 1)
                    act.wait_ge(turned, k + 1)
                    act.wait_ge(xt_out[s], i * 16)
                    for c in range(DC):
                        last = nc.scalar.activation(xt[s][:, c, :], psum[:, 1 + 2 * s + c, :], ACT.Copy)
                    last.then_inc(turned_copied, 1)


def rank(nc, b):
    sem, carve, psum = b.sem, b.carve, b.psum
    hi_all = carve(0, [ECOLS + SUPER], BF16)
    at = (ECOLS + SUPER) // 2
    places = carve(at, [ECOLS])
    at += ECOLS
    hot = [carve(at, [SUPER, P], BF16),
           b.xnt[:].rearrange("p c m -> p (c m)").bitcast(BF16)[:, 0:SUPER * P].rearrange("p (j c) -> p j c", c=P)]
    at += SUPER * P // 2 - 2048
    count_bf = carve(at + 3072, [P], BF16)
    base_i = carve(at + 3136, [P], I32)
    digit_i = carve(at + 3264, [P], I32)
    digits = carve(at + 3392, [2, P], BF16)
    fold = carve(at + 2048, [8])
    spread = carve(at + 2056, [16, 8])
    masked = carve(at + 2184, [64])
    total = carve(at + 2248, [P], I32)
    chunks = carve(at + 2376, [P])
    ends = carve(at + 2504, [P])
    starts = carve(at + 2632, [P])
    carry = carve(at + 2760, [2, P])
    loops_f = carve(at + 3016, [2])
    loops_i = carve(at + 3018, [2], I32)
    tile_f = carve(at + 3020, [CHUNK_COLS])
    tile_i = carve(at + 3040, [CHUNK_COLS], I32)
    quarter = ECOLS // 4
    over = b.xnt[:, 0, 0:quarter]
    place_i = b.xnt[:, 1, :].bitcast(I32).rearrange("p (s n) -> p s n", s=2)
    window = b.order_bf[:, 0:2 * P - 1]
    lies_before = b.order_bf[:, C_BEFORE - C_WINDOW:C_PICK - C_WINDOW]
    pick = b.order_bf[0:3 * GROUPS, C_PICK - C_WINDOW:C_ALL - C_WINDOW]
    before = b.xnt[:, 0, :].rearrange("p (a c) -> p a c", c=P)[:, 0:CHUNK_COLS, :]

    dve_step, fold_ready, totals_ready, base_ready = (
        sem("dve_step_rank"), sem("fold_ready"), sem("totals_ready"), sem("base_ready"))
    small_out, place_out = sem("small_out"), [sem(f"place_out{s}") for s in range(2)]
    place_made, small_made = sem("place_made"), sem("small_made")
    hot_ready, count_ready, count_copied, base_sum_ready, carry_sum_ready, carry_ready = (
        sem("rank_hot_ready"), sem("count_ready"), sem("count_copied"), sem("base_sum_ready"),
        sem("carry_sum_ready"), sem("carry_ready"))
    digit_step, rank_ready, rank_used = sem("digit_step"), sem("rank_ready"), sem("rank_used")
    SUPERS = ECOLS // SUPER

    with nc.Block() as block:
        @block.vector
        def _(dve):
            t = Tally(dve, dve_step)
            t.then(nc.vector.tensor_tensor(masked, b.counts[:], b.cst[:, C_DIAG:C_DIAG + 64], ALU.mult))
            t.then(nc.vector.tensor_reduce(fold, masked.rearrange("p (j l) -> p l j", l=8), AX.X, ALU.add))
            nc.vector.tensor_tensor(spread, fold.unsqueeze(1).broadcast_to([P, 16, 8]),
                                    b.cst[:, C_FOLD:C_FOLD + 16].unsqueeze(2).broadcast_to([P, 16, 8]),
                                    ALU.mult).then_inc(fold_ready, 1)
            dve.wait_ge(totals_ready, 1)
            t.then(nc.vector.tensor_scalar(total, psum[:, 0, 0:P], float(CHUNK - 1), None, ALU.add))
            t.then(nc.vector.tensor_scalar(total, total, CHUNK.bit_length() - 1, None, ALU.logical_shift_right))
            t.then(nc.vector.tensor_copy(chunks, total))
            t.then(nc.vector.tensor_tensor_scan(ends, chunks, chunks, 0.0, ALU.add, ALU.bypass))
            t.then(nc.vector.tensor_tensor(starts, ends, chunks, ALU.subtract))
            nc.vector.tensor_scalar(carry[:, 0, :], starts, float(CHUNK), None, ALU.mult).then_inc(base_ready, 1)
            t.then(nc.vector.tensor_scalar(loops_f[:, 1:2], ends[:, P - 1:P], float(SUM_SLOTS - 1), float(SUM_SLOTS),
                                           ALU.add, ALU.max))
            t.then(nc.vector.tensor_copy(loops_i[:, 1:2], loops_f[:, 1:2]))
            t.then(nc.vector.tensor_scalar(loops_i[:, 1:2], loops_i[:, 1:2], SUM_SLOTS.bit_length() - 1, None,
                                           ALU.logical_shift_right))
            t.then(nc.vector.tensor_scalar(loops_i[:, 0:1], loops_i[:, 1:2], float(SUM_SLOTS // 2), None, ALU.mult))
            t.then(nc.vector.tensor_tensor(before, ends.unsqueeze(1).broadcast_to([P, CHUNK_COLS, P]),
                                           b.cst[:, C_CID:C_CID + CHUNK_COLS].unsqueeze(2).broadcast_to(
                                               [P, CHUNK_COLS, P]), ALU.is_le))
            t.then(nc.vector.tensor_reduce(tile_f, before, AX.X, ALU.add))
            nc.vector.tensor_scalar(tile_i, tile_f, float(TILES - 1), None, ALU.min).then_inc(small_made, 1)

            def one_hot(slot, n, super_):
                for j in range(4 * n, 4 * n + 4):
                    last = nc.vector.tensor_scalar(hot[slot][:, j, :], b.iota_bf[:],
                                                   hi_all[:, bass.ds(super_ * SUPER + j, 1)], None, ALU.is_equal)
                last.then_inc(hot_ready, 1)

            for n in range(GROUPS):
                one_hot(0, n, 0)
            with dve.Fori(0, SUPERS // 2) as i:
                for s in range(2):
                    k = i * 2 + s
                    dve.wait_ge(base_sum_ready, k + 1)
                    t = Tally(dve, digit_step, base=k * 5)
                    t.then(nc.vector.tensor_copy(base_i[0:3 * GROUPS, :], psum[0:3 * GROUPS, 6, 0:P]))
                    for d in range(3):
                        r = slice(d * GROUPS, (d + 1) * GROUPS)
                        t.then(nc.vector.tensor_scalar(digit_i[r, :], base_i[r, :], 8 * d, 255,
                                                       ALU.logical_shift_right, ALU.bitwise_and))
                    t.mark(nc.vector.tensor_copy(digits[0:3 * GROUPS, s, :], digit_i[0:3 * GROUPS, :]))
                    for g in range(GROUPS):
                        one_hot(1 - s, g, k + 1)
                        dve.wait_ge(rank_ready, k * GROUPS + g + 1)
                        nc.vector.tensor_reduce(places[:, bass.ds(k * SUPER + g * 4, 4)],
                                                psum[:, g % 4, :].rearrange("p (q c) -> p q c", c=P), AX.X,
                                                ALU.max).then_inc(rank_used, 1)
            dve.wait_ge(rank_used, SUPERS * GROUPS)
            for n in range(4):
                v = places[:, n * quarter:(n + 1) * quarter]
                t.then(nc.vector.tensor_scalar(over, v, BIG, 2.0 * BIG, ALU.is_lt, ALU.mult))
                if n >= 2:
                    dve.wait_ge(place_out[n % 2], 16)
                nc.vector.scalar_tensor_tensor(place_i[:, n % 2, :], v, -BIG, over, ALU.add, ALU.add).then_inc(
                    place_made, 1)
                dve.wait_ge(place_made, n + 1)

        @block.tensor
        def _(pe):
            pe.wait_ge(fold_ready, 1)
            nc.tensor.matmul(psum[:, 0, 0:P], b.ones, spread.rearrange("p a c -> p (a c)"), start=True,
                             stop=True).then_inc(totals_ready, 1)
            pe.wait_ge(base_ready, 1)

            def count(slot, g, bank):
                for j in range(4 * g, 4 * g + 4):
                    last = nc.tensor.matmul(psum[:, bank, 0:P], window[:, P - 1 - j:2 * P - 1 - j], hot[slot][:, j, :],
                                            start=(j == 0), stop=(j == SUPER - 1))
                return last

            def bases(k, s):
                pe.wait_ge(count_copied, k + 1)
                pe.wait_ge(carry_ready, k)
                nc.tensor.matmul(psum[0:3 * GROUPS, 6, 0:P], lies_before, count_bf, start=True, stop=False)
                nc.tensor.matmul(psum[0:3 * GROUPS, 6, 0:P], b.ones[0:1, 0:3 * GROUPS], carry[0:1, s, :], start=False,
                                 stop=True).then_inc(base_sum_ready, 1)
                nc.tensor.matmul(psum[0:1, 7, 0:P], b.ones_bf[:, 0:1], count_bf, start=True, stop=False)
                nc.tensor.matmul(psum[0:1, 7, 0:P], b.ones[0:1, 0:1], carry[0:1, s, :], start=False,
                                 stop=True).then_inc(carry_sum_ready, 1)

            def ranks(k, s, first):
                bases(k, s)
                pe.wait_ge(digit_step, (k + 1) * 5)
                for g in range(GROUPS):
                    hs = hot[s][:, 4 * g:4 * g + 4, :]
                    out = psum[:, g % 4, :]
                    if not first or g >= 4:
                        pe.wait_ge(rank_used, k * GROUPS + (g - 3) if g >= 3 else k * GROUPS - (3 - g))
                    nc.tensor.matmul(out, pick[:, g:g + 1].broadcast_to([3 * GROUPS, P]),
                                     digits[0:3 * GROUPS, s, :].unsqueeze(1).broadcast_to([3 * GROUPS, 4, P]),
                                     start=True, stop=False)
                    for q in range(3):
                        nc.tensor.matmul(out[:, (q + 1) * P:], b.ones_bf[:],
                                         hs[:, q:q + 1, :].broadcast_to([P, 3 - q, P]), start=False, stop=False)
                    nc.tensor.matmul(out, b.rank_bf[:], hs, start=False, stop=True).then_inc(rank_ready, 1)
                    pe.wait_ge(hot_ready, (k + 1) * GROUPS + (g + 1))
                    last = count(1 - s, g, 4 + (1 - s))
                last.then_inc(count_ready, 1)

            for g in range(GROUPS):
                pe.wait_ge(hot_ready, g + 1)
                last = count(0, g, 4)
            last.then_inc(count_ready, 1)
            ranks(0, 0, True)
            ranks(1, 1, False)
            with pe.Fori(1, SUPERS // 2) as i:
                for s in range(2):
                    ranks(i * 2 + s, s, False)

        @block.scalar
        def _(act):
            with act.Fori(0, SUPERS // 2) as i:
                for s in range(2):
                    k = i * 2 + s
                    act.wait_ge(count_ready, k + 1)
                    act.wait_ge(carry_sum_ready, k)
                    nc.scalar.activation(count_bf, psum[:, 4 + s, 0:P], ACT.Copy).then_inc(count_copied, 1)
                    act.wait_ge(carry_sum_ready, k + 1)
                    nc.scalar.activation(carry[0:1, 1 - s, :], psum[0:1, 7, 0:P], ACT.Copy).then_inc(carry_ready, 1)

        @block.sync
        def _(sp):
            sp.wait_ge(small_made, 1)
            with nc.allow_non_contiguous_dma("a few words"):
                sp.dma_start(b.chunk_tile_d.rearrange("q p -> p q"), tile_i).then_inc(small_out, 16)
            sp.dma_start(b.loops_d[:, :], loops_i[0:1, :]).then_inc(small_out, 16)
            for n in range(4):
                sp.wait_ge(place_made, n + 1)
                sp.dma_start(b.place_d[:, n * quarter:(n + 1) * quarter], place_i[:, n % 2, :]).then_inc(
                    place_out[n % 2], 16)
            sp.wait_ge(small_out, 32)
            for s in range(2):
                sp.wait_ge(place_out[s], 32)


def pool_rows(nc, b):
    sem, carve, psum, sb = b.sem, b.carve, b.psum, b.sb
    half = [[b.arena[:, (2 * n + g) * M:(2 * n + g + 1) * M] for g in range(2)] for n in range(2)]
    fresh = [b.arena[:, (4 + g) * M:(5 + g) * M] for g in range(2)]
    done = half[(N_STAGES - 1) % 2]

    rows = sb("rows", [P, DC, 2 * P], F32)
    resid = sb("resid", [P, 2, D], F32)
    pooled = sb("pooled", [P, 2, D], F32)
    x2 = sb("x2", [P, 2, D], F32)
    tn = sb("tn", [P, 2, D], F32)
    tt = sb("tt", [P, DC, 2 * P], F32)
    tab = sb("tab", [P, 2, TAB], F32)
    hid = sb("hid", [P, 2, HC, 2 * P], F32)
    ys = sb("ys", [P, 2, 2, D], F32)
    stat = sb("stat", [P, 2, 6], F32)
    mv = sb("mv", [P, 2, 2], F32)
    std = sb("std", [P, 2], F32)
    var = sb("var", [P, 2], F32)
    rs = sb("rs", [P, 2], F32)
    rt = sb("rt", [P, 2], F32)
    word_s = sb("word_s", [P, 2, SCAT], I32)
    place_s = sb("place_s", [P, 2, SCAT], I32)

    xnt_in, rows_in = sem("xnt_in"), sem("rows_in")
    corr_ready, corr_copied = sem("corr_ready"), sem("corr_copied")
    sorted_ = [sem(f"sorted{g}") for g in range(2)]
    carried = [sem(f"carried{g}") for g in range(2)]
    picked, resid_in, x2_ready, x2_out = sem("picked"), sem("resid_in"), sem("x2_ready"), sem("x2_out")
    std_ready, tn_ready, tn_turned, tt_ready = sem("std2_ready"), sem("tn_ready"), sem("tn_turned"), sem("tt_ready")
    tab_ready, tab_copied, tab_out = sem("tab_ready"), sem("tab_copied"), sem("tab_out")
    hid_ready, gelu_ready, y_ready, y_copied = sem("hid_ready"), sem("gelu_ready"), sem("y_ready"), sem("y_copied")
    y_out = [sem(f"y_out{s}") for s in range(2)]
    dve_step = sem("dve_step_pool")
    pool_in = [sem(f"pool_in{s}") for s in range(2)]
    scattered = [sem(f"scattered{s}") for s in range(SCAT_SEMS)]

    x_p = b.x_t.rearrange("(i g) p d -> i p g d", g=2)
    x2_p = b.x2_d.rearrange("(i g) p d -> i p g d", g=2)
    y_p = b.y_d.rearrange("(i g) p (e d) -> i p e g d", g=2, e=EXPERTS)
    tab_p = b.table_d.rearrange("(i g p) f -> i p g f", g=2, p=P)

    def of(view, i):
        return view[bass.ds(i, 1)].rearrange("o p g d -> (o p) g d")

    ADD_AT, NORM_AT = 4, 8
    TURN_AT, EXPERT_AT, COPY_AT = 10, 14, 34
    STEPS = 8

    with nc.Block() as block:
        @block.sync
        def _(sp):
            sp.dma_start(b.xnt[:], b.xnt_d[:, :, 0:M]).then_inc(xnt_in, 16)

            def load_rows(i):
                sp.wait_ge(corr_ready, i * (2 * CORR_CHUNKS))
                sp.dma_start(rows[:], b.xnt_d[:, :, bass.ds(i * (2 * P), 2 * P)]).then_inc(rows_in, 16)

            def stores(i):
                if not (isinstance(i, int) and i >= PAIRS - 2):
                    load_rows(i + 2)
                sp.wait_ge(x2_ready, i + 1)
                sp.dma_start(of(x2_p, i), x2[:]).then_inc(x2_out, 16)
                sp.wait_ge(tab_copied, i + 1)
                sp.dma_start(of(tab_p, i), tab[:]).then_inc(tab_out, 16)
                for e in range(EXPERTS):
                    sp.wait_ge(y_copied, i * EXPERTS + (e + 1))
                    sp.dma_start(of(y_p[:, :, e], i), ys[:, e % 2]).then_inc(y_out[e % 2], 16)
                nxt = (i + 1) % PAIRS
                sp.dma_start(resid[:], of(x_p, nxt)).then_inc(resid_in, 16)

            load_rows(0)
            sp.dma_start(resid[:], of(x_p, 0)).then_inc(resid_in, 16)
            load_rows(1)
            for image in range(1, IMAGES + 1):
                if image > 1:
                    with sp.Fori(PAIRS_OF_IMAGE * (image - 1) - 1, PAIRS_OF_IMAGE * image - 2) as i:
                        stores(i)
                else:
                    with sp.Fori(0, PAIRS_OF_IMAGE - 2) as i:
                        stores(i)
                stores(PAIRS_OF_IMAGE * image - 2)
                if image < IMAGES:
                    sp.wait_ge(corr_ready, PAIRS_OF_IMAGE * image * 2 * CORR_CHUNKS)
                    sp.dma_start(b.xnt[:], b.xnt_d[:, :, image * M:(image + 1) * M]).then_inc(xnt_in, 16)
            stores(PAIRS - 1)
            sp.wait_ge(resid_in, 16 * (PAIRS + 1))
            sp.wait_ge(x2_out, 16 * PAIRS)
            sp.wait_ge(tab_out, 16 * PAIRS)
            for s in range(2):
                sp.wait_ge(y_out[s], 16 * PAIRS * EXPERTS // 2)

        @block.tensor
        def _(pe):
            def correlate(i):
                pe.wait_ge(xnt_in, (i // PAIRS_OF_IMAGE + 1) * 16)
                pe.wait_ge(rows_in, (i + 1) * 16)
                for g in range(2):
                    for n in range(CORR_CHUNKS):
                        k = i * (2 * CORR_CHUNKS) + (g * CORR_CHUNKS + n)
                        if not (isinstance(i, int) and i == 0 and g == 0 and n < 2):
                            pe.wait_ge(corr_copied, k - 1)
                        for c in range(DC):
                            last = nc.tensor.matmul(psum[:, n % 2, :], rows[:, c, g * P:(g + 1) * P],
                                                    b.xnt[:, c, n * BANK:(n + 1) * BANK], start=(c == 0),
                                                    stop=(c == DC - 1))
                        last.then_inc(corr_ready, 1)

            def experts(i):
                pe.wait_ge(tn_ready, i + 1)
                for c in range(DC):
                    for g in range(2):
                        last = nc.tensor.transpose(psum[:, 2, (2 * c + g) * P:(2 * c + g + 1) * P],
                                                   tn[:, g, c * P:(c + 1) * P], b.ident)
                last.then_inc(tn_turned, 1)
                pe.wait_ge(tt_ready, i + 1)
                for g in range(2):
                    for c in range(DC):
                        last = nc.tensor.matmul(psum[:, 3, g * TAB:(g + 1) * TAB], tt[:, c, g * P:(g + 1) * P],
                                                b.wtab[:, c, :], start=(c == 0), stop=(c == DC - 1))
                last.then_inc(tab_ready, 1)

                def down(e):
                    pe.wait_ge(gelu_ready, (i * EXPERTS + (e + 1)) * HC)
                    for g in range(2):
                        if e > 0 or not (isinstance(i, int) and i == 0):
                            pe.wait_ge(y_copied, i * EXPERTS + e)
                        for m in range(HC):
                            nc.tensor.matmul(psum[:, 6 + g, 0:D], hid[:, e % 2, m, g * P:(g + 1) * P],
                                             b.w2s[:, e, m, :], start=(m == 0), stop=False)
                        last = nc.tensor.matmul(psum[:, 6 + g, 0:D], b.ones[0:1, :], b.b2s[0:1, e * D:(e + 1) * D],
                                                start=False, stop=True)
                    last.then_inc(y_ready, 1)

                for e in range(EXPERTS):
                    for m in range(HC):
                        k = (i * EXPERTS + e) * HC + m
                        if not (isinstance(k, int) and k < 2):
                            pe.wait_ge(gelu_ready, k - 1)
                        for c in range(DC):
                            last = nc.tensor.matmul(psum[:, 4 + m % 2, 0:2 * P], b.w1s[:, e, c, m * P:(m + 1) * P],
                                                    tt[:, c, :], start=(c == 0), stop=(c == DC - 1))
                        last.then_inc(hid_ready, 1)
                    if e > 0:
                        down(e - 1)
                down(EXPERTS - 1)

            correlate(0)
            correlate(1)
            experts(0)
            correlate(2)
            with pe.Fori(2, PAIRS - 1) as i:
                experts(i - 1)
                correlate(i + 1)
            experts(PAIRS - 2)
            experts(PAIRS - 1)

        @block.vector
        def _(dve):
            def residual(i):
                dve.wait_ge(picked, i + 1)
                dve.wait_ge(resid_in, (i + 1) * 16)
                dve.wait_ge(x2_out, i * 16)
                t = Tally(dve, dve_step, base=i * STEPS)
                t.then(nc.vector.tensor_tensor(x2[:], resid[:], pooled[:], ALU.add))
                for g in range(2):
                    last = nc.vector.bn_stats(stat[:, g, :], x2[:, g, :])
                last.then_inc(x2_ready, 1)
                dve.wait_ge(x2_ready, i + 1)
                dve.sem_inc(b.settled[0], 1)
                for g in range(2):
                    last = nc.vector.bn_aggr(mv[:, g, :], stat[:, g, :])
                t.then(last)
                t.mark(nc.vector.tensor_scalar(var[:], mv[:, :, 1], LN_T_EPS, None, ALU.add))

            def normalise(i):
                dve.wait_ge(std_ready, i + 1)
                t = Tally(dve, dve_step, base=i * STEPS + 3)
                newton(nc, t, rs[:], rt[:], var[:], std[:])
                dve.wait_ge(tn_turned, i)
                for g in range(2):
                    last = nc.vector.tensor_scalar(tn[:, g, :], x2[:, g, :], mv[:, g, 0:1], rs[:, g:g + 1],
                                                   ALU.subtract, ALU.mult)
                last.then_inc(tn_ready, 1)

            def sort(i, after_first):
                n_carried = 0
                done_before = i * N_STAGES
                carried_before = i * N_CARRIED
                for s, (p, k) in enumerate(STAGES):
                    for g in range(2):
                        source = fresh[g] if s == 0 else half[(s - 1) % 2][g]
                        hi_in, lo_in, _ = compared(source, p, k)
                        hi_out, lo_out, _ = compared(half[s % 2][g], p, k)
                        if s == 0:
                            dve.wait_ge(corr_copied, i * (2 * CORR_CHUNKS) + (g + 1) * CORR_CHUNKS)
                        if s > 0 or after_first:
                            dve.wait_ge(sorted_[g], done_before + s)
                            dve.wait_ge(carried[g], carried_before + n_carried)
                        if s == 1 and after_first:
                            dve.wait_ge(picked, i)
                        nc.vector.tensor_tensor(hi_out, hi_in, lo_in, ALU.max)
                        nc.vector.tensor_tensor(lo_out, hi_in, lo_in, ALU.min).then_inc(sorted_[g], 1)
                    n_carried += k < p
                    if after_first and s == ADD_AT:
                        residual(i - 1)
                    if after_first and s == NORM_AT:
                        normalise(i - 1)

            sort(0, False)
            with dve.Fori(1, PAIRS) as i:
                sort(i, True)
            residual(PAIRS - 1)
            normalise(PAIRS - 1)

        @block.scalar
        def _(act):
            def evacuate(i, g, n):
                act.wait_ge(corr_ready, i * (2 * CORR_CHUNKS) + (g * CORR_CHUNKS + n + 1))
                if n == 0 and not (isinstance(i, int) and i == 0):
                    act.wait_ge(sorted_[g], (i - 1) * N_STAGES + 1)
                nc.scalar.activation(fresh[g][:, n * BANK:(n + 1) * BANK], psum[:, n % 2, :], ACT.Copy,
                                     scale=1.0 / D).then_inc(corr_copied, 1)

            def pick(i):
                if not (isinstance(i, int) and i == 0):
                    act.wait_ge(x2_ready, i)
                for g in range(2):
                    act.wait_ge(sorted_[g], (i + 1) * N_STAGES)
                    act.wait_ge(carried[g], (i + 1) * N_CARRIED)
                    for first, r, count in RUNS:
                        last = nc.scalar.activation(pooled[:, g, first:first + count],
                                                    done[g][:, r:r + 16 * (count - 1) + 1:16], ACT.Copy)
                last.then_inc(picked, 1)

            def deviation(i):
                act.wait_ge(dve_step, i * STEPS + 3)
                nc.scalar.activation(std[:], var[:], ACT.Sqrt).then_inc(std_ready, 1)

            def turn(i):
                act.wait_ge(tn_turned, i + 1)
                if not (isinstance(i, int) and i == 0):
                    act.wait_ge(y_ready, i * EXPERTS)
                nc.scalar.activation(tt[:].rearrange("p c t -> p (c t)"), psum[:, 2, :], ACT.Copy).then_inc(tt_ready, 1)
                act.wait_ge(tab_ready, i + 1)
                act.wait_ge(tab_out, i * 16)
                nc.scalar.activation(tab[:].rearrange("p g f -> p (g f)"), psum[:, 3, 0:2 * TAB], ACT.Copy).then_inc(
                    tab_copied, 1)

            def hidden(i, e):
                for m in range(HC):
                    act.wait_ge(hid_ready, (i * EXPERTS + e) * HC + (m + 1))
                    if m == 0:
                        k = i * EXPERTS + e
                        if not (isinstance(k, int) and k < 2):
                            act.wait_ge(y_ready, k - 1)
                    nc.scalar.activation(hid[:, e % 2, m, :], psum[:, 4 + m % 2, 0:2 * P], ACT.Gelu,
                                         bias=b.b1s[:, e, m:m + 1]).then_inc(gelu_ready, 1)

            def expert_out(i, e):
                act.wait_ge(y_ready, i * EXPERTS + (e + 1))
                act.wait_ge(y_out[e % 2], (i * 2 + e // 2) * 16)
                nc.scalar.activation(ys[:, e % 2], psum[:, 6:8, 0:D], ACT.Copy).then_inc(y_copied, 1)

            def experts(i, part):
                if part < EXPERTS:
                    hidden(i, part)
                if part > 0:
                    expert_out(i, part - 1)

            def carry_over(i, after_first, before_last):
                n_carried = 0
                done_before = i * N_STAGES
                carried_before = i * N_CARRIED
                if after_first:
                    pick(i - 1)
                for s, (p, k) in enumerate(STAGES):
                    if k < p:
                        for g in range(2):
                            _, _, same_in = compared(half[(s - 1) % 2][g], p, k)
                            _, _, same_out = compared(half[s % 2][g], p, k)
                            act.wait_ge(sorted_[g], done_before + s)
                            act.wait_ge(carried[g], carried_before + n_carried)
                            nc.scalar.activation(same_out[0], same_in[0], ACT.Copy)
                            nc.scalar.activation(same_out[1], same_in[1], ACT.Copy).then_inc(carried[g], 1)
                        n_carried += 1
                    if after_first:
                        if s == NORM_AT - 1:
                            deviation(i - 1)
                        if s == TURN_AT:
                            turn(i - 1)
                        if s >= EXPERT_AT and (s - EXPERT_AT) % 4 == 0 and (s - EXPERT_AT) // 4 <= EXPERTS:
                            experts(i - 1, (s - EXPERT_AT) // 4)
                    if before_last and s >= COPY_AT and s < COPY_AT + 4 * CORR_CHUNKS and (s - COPY_AT) % 2 == 0:
                        n = (s - COPY_AT) // 2
                        evacuate(i + 1, n // CORR_CHUNKS, n % CORR_CHUNKS)

            for g in range(2):
                for n in range(CORR_CHUNKS):
                    evacuate(0, g, n)
            carry_over(0, False, True)
            carry_over(1, True, True)
            with act.Fori(2, PAIRS - 1) as i:
                carry_over(i, True, True)
            carry_over(PAIRS - 1, True, False)
            pick(PAIRS - 1)
            deviation(PAIRS - 1)
            turn(PAIRS - 1)
            for part in range(EXPERTS + 1):
                experts(PAIRS - 1, part)

        @block.gpsimd
        def _(pool):
            per_sem = SCAT // SCAT_SEMS
            with pool.Fori(0, ECOLS // SCAT // 2) as i:
                for s in range(2):
                    for k in range(SCAT_SEMS):
                        pool.wait_ge(scattered[k], i * (2 * per_sem * 16) + (s * per_sem * 16 if s else 0))
                    pool.sem_inc(b.settled[1], 1)
                    col = (i * 2 + s) * SCAT
                    pool.dma_start(word_s[:, s, :], b.words_d[:, bass.ds(col, SCAT)]).then_inc(pool_in[s], 16)
                    pool.dma_start(place_s[:, s, :], b.place_d[:, bass.ds(col, SCAT)]).then_inc(pool_in[s], 16)
                    pool.wait_ge(pool_in[s], (i + 1) * 32)
                    pool.sem_inc(b.settled[1], 1)
                    for j in range(SCAT):
                        pool.indirect_dma_start(
                            out=b.sorted_d[:, :], out_offset=bass.IndirectOffsetOnAxis(ap=place_s[:, s, j:j + 1], axis=0),
                            in_=word_s[:, s, j:j + 1], in_offset=None, bounds_check=CAPACITY - 1,
                            oob_is_err=False).then_inc(scattered[j % SCAT_SEMS], 16)
            for k in range(SCAT_SEMS):
                pool.wait_ge(scattered[k], ECOLS // SCAT_SEMS * 16)


def newton(nc, t, r, tmp, v, std):
    t.then(nc.vector.reciprocal(r, std))
    t.then(nc.vector.tensor_tensor(tmp, r, r, ALU.mult))
    t.then(nc.vector.tensor_tensor(tmp, tmp, v, ALU.mult))
    t.then(nc.vector.tensor_scalar(tmp, tmp, -0.5, 1.5, ALU.mult, ALU.add))
    t.then(nc.vector.tensor_tensor(r, r, tmp, ALU.mult))


def segment_max(nc, b):
    sem, carve, psum = b.sem, b.carve, b.psum
    table = carve(0, [TILES, TAB])
    top = carve(TILES * TAB, [TILES, HEADS])
    at = TILES * (TAB + HEADS)
    tiles_i = carve(at, [CHUNK_COLS * P], I32)
    loops_i = carve(at + CHUNK_COLS * P, [2], I32)
    at += CHUNK_COLS * P + 8
    word = [carve(at + 16 * s, [EQ], I32) for s in range(2)]
    source = [carve(at + 16 * s + 4, [EQ], I32) for s in range(2)]
    low = [carve(at + 16 * s + 8, [EQ], I32) for s in range(2)]
    best = [carve(at + 16 * s + 12, [HEADS]) for s in range(2)]
    got = [carve(at + 32 + 96 * s, [EQ, TAB]) for s in range(2)]
    other = [carve(at + 224 + 512 * s, [EQ, P]) for s in range(2)]
    spread = [carve(at + 1248 + 2048 * s, [HEADS, EQ, P]) for s in range(2)]

    setup_in, word_in, store_out = (sem("max_setup_in"), [sem(f"word_in{s}") for s in range(2)],
                                    [sem(f"gathered_out{s}") for s in range(2)])
    got_in = [[sem(f"got_in{s}_{q}") for q in range(EQ)] for s in range(2)]
    source_ready, spread_ready, turned, best_ready, dve_step = (
        sem("source_ready"), sem("spread_ready"), sem("max_turned"), sem("best_ready"), sem("dve_step_max"))
    loaded = sem("max_loaded")
    sorted_c = b.sorted_d.rearrange("(c p q) o -> c p (q o)", p=P, q=EQ)

    def chunk(view, c):
        return view[bass.ds(c, 1)].rearrange("o p q -> (o p) q")

    with nc.Block() as block:
        @block.sync
        def _(sp):
            sp.dma_start(tiles_i[0:1, :], b.chunk_tile_d.rearrange("q p -> (q p)").rearrange("(o k) -> o k", o=1)
                         ).then_inc(setup_in, 16)
            sp.dma_start(loops_i[0:1, :], b.loops_d[:, :]).then_inc(setup_in, 16)
            sp.dma_start(table, b.table_d.rearrange("(t p) f -> p t f", p=P)).then_inc(setup_in, 16)
            for s in range(2):
                sp.dma_start(word[s], sorted_c[s]).then_inc(word_in[s], 16)
            sp.wait_ge(setup_in, 48)
            pairs = sp.value_load(loops_i[0:1, 0:1], min_val=1, max_val=MOST_PAIRS)
            with sp.Fori(0, pairs) as i:
                for s in range(2):
                    sp.wait_ge(source_ready, i * 2 + (s + 1))
                    sp.dma_start(word[s], chunk(sorted_c, i * 2 + (s + 2))).then_inc(word_in[s], 16)
                for s in range(2):
                    for q in range(EQ):
                        sp.wait_ge(got_in[s][q], (i + 1) * 16)
                    sp.dma_start(chunk(b.gathered_d, i * 2 + s), got[s].rearrange("p q f -> p (q f)")).then_inc(
                        store_out[s], 16)
            for s in range(2):
                sp.wait_ge(word_in[s], (pairs + 1) * 16)
                sp.sem_inc(b.settled[2], 1)
                sp.wait_ge(store_out[s], pairs * 16)
                sp.sem_inc(b.settled[2], 1)

        @block.vector
        def _(dve):
            def take_apart(i, s):
                dve.wait_ge(word_in[s], (i + 1) * 16)
                nc.vector.tensor_scalar(source[s], word[s], 8, None, ALU.logical_shift_right)
                nc.vector.tensor_scalar(low[s], word[s], 255, None, ALU.bitwise_and).then_inc(source_ready, 1)
                dve.wait_ge(source_ready, i * 2 + (s + 1))
                nc.vector.tensor_tensor(other[s], b.iota.unsqueeze(1).broadcast_to([P, EQ, P]),
                                        low[s].unsqueeze(2).broadcast_to([P, EQ, P]),
                                        ALU.not_equal).then_inc(dve_step, 1)
                dve.wait_ge(dve_step, (i * 2 + s) * 2 + 1)
                nc.vector.tensor_scalar(other[s], other[s], MASKED, None, ALU.mult).then_inc(dve_step, 1)

            dve.wait_ge(setup_in, 48)
            pairs = dve.value_load(loops_i[0:1, 0:1], min_val=1, max_val=MOST_PAIRS)
            nc.vector.tensor_copy(top, table[:, :, 0:HEADS]).then_inc(best_ready, 1)
            for s in range(2):
                take_apart(0, s)
            with dve.Fori(0, pairs) as i:
                for s in range(2):
                    for q in range(EQ):
                        dve.wait_ge(got_in[s][q], (i + 1) * 16)
                    dve.wait_ge(dve_step, i * 4 + (2 * s + 2))
                    dve.wait_ge(turned, i * 2)
                    nc.vector.tensor_tensor(
                        spread[s], other[s].unsqueeze(1).broadcast_to([P, HEADS, EQ, P]),
                        got[s][:, :, 0:HEADS].rearrange("p q h -> p h q").unsqueeze(3).broadcast_to(
                            [P, HEADS, EQ, P]), ALU.add).then_inc(spread_ready, 1)
                    dve.wait_ge(spread_ready, i * 2 + (s + 1))
                    take_apart(i + 1, s)
                for s in range(2):
                    dve.wait_ge(turned, i * 2 + (s + 1))
                    tile = dve.value_load(tiles_i[0:1, bass.ds(i * 2 + s, 1)], min_val=0, max_val=TILES - 1)
                    nc.vector.tensor_reduce(best[s], psum[:, 4 * s:4 * s + 4, :], AX.X, ALU.max).then_inc(
                        best_ready, 1)
                    dve.wait_ge(best_ready, i * 4 + (2 * s + 2))
                    t = top[:, bass.ds(tile, 1), :].rearrange("p o h -> p (o h)")
                    nc.vector.tensor_tensor(t, t, best[s], ALU.max).then_inc(best_ready, 1)

        @block.tensor
        def _(pe):
            pe.wait_ge(setup_in, 48)
            pairs = pe.value_load(loops_i[0:1, 0:1], min_val=1, max_val=MOST_PAIRS)
            with pe.Fori(0, pairs) as i:
                for s in range(2):
                    pe.wait_ge(spread_ready, i * 2 + (s + 1))
                    pe.wait_ge(best_ready, i * 4 + (2 * s - 2 if s else 0))
                    for h in range(HEADS):
                        for q in range(EQ):
                            last = nc.tensor.transpose(psum[:, 4 * s + h, q * P:(q + 1) * P], spread[s][:, h, q, :],
                                                       b.ident)
                    last.then_inc(turned, 1)

        @block.gpsimd
        def _(pool):
            pool.wait_ge(setup_in, 48)
            pairs = pool.value_load(loops_i[0:1, 0:1], min_val=1, max_val=MOST_PAIRS)
            with pool.Fori(0, pairs) as i:
                for s in range(2):
                    pool.wait_ge(source_ready, i * 2 + (s + 1))
                    pool.wait_ge(spread_ready, (i * 2 + s) if s == 0 else i * 2)
                    pool.wait_ge(store_out[s], i * 16)
                    pool.sem_inc(b.settled[1], 1)
                    for q in range(EQ):
                        pool.indirect_dma_start(
                            out=got[s][:, q, :], out_offset=None, in_=b.table_d[:, :],
                            in_offset=bass.IndirectOffsetOnAxis(ap=source[s][:, q:q + 1], axis=0),
                            bounds_check=TOKENS - 1, oob_is_err=False).then_inc(got_in[s][q], 16)


def segment_sum(nc, b):
    sem, carve, psum = b.sem, b.carve, b.psum
    W = HEADS + GAT
    table = carve(0, [TILES, TAB])
    top = carve(TILES * TAB, [TILES, HEADS])
    at = TILES * (TAB + HEADS)
    sums = carve(at, [TILES, W])
    info = carve(at + TILES * W, [TILES, 2 * HEADS])
    at += TILES * (W + 2 * HEADS)
    tiles_i = carve(at, [CHUNK_COLS * P], I32)
    loops_i = carve(at + CHUNK_COLS * P, [2], I32)
    at += CHUNK_COLS * P + 8
    raw = carve(at, [TILES, HEADS])
    at += TILES * HEADS
    R = range(SUM_SLOTS)
    word = [carve(at + 64 * s, [EQ], I32) for s in R]
    low = [carve(at + 64 * s + 4, [EQ], I32) for s in R]
    z = [carve(at + 64 * s + 8, [EQ, HEADS]) for s in R]
    at += 64 * SUM_SLOTS
    got = [carve(at + 96 * s, [EQ, TAB]) for s in R]
    at += 96 * SUM_SLOTS
    value = [carve(at + 80 * s, [EQ, W]) for s in R]
    at += 80 * SUM_SLOTS
    hot = [carve(at + 512 * s, [EQ, P]) for s in R]
    at += 512 * SUM_SLOTS
    hot_t = [carve(at + 512 * s, [EQ, P]) for s in R]
    at += 512 * SUM_SLOTS
    assert at <= 6 * M

    sem_ = lambda n: sem("sum_" + n)
    setup_in, chunk_in = sem_("setup_in"), [sem_(f"chunk_in{s}") for s in R]
    info_step, low_ready, hot_ready, turned, copied, looked_up, z_step, exp_ready, value_ready, summed, added = (
        sem_("info_step"), sem_("low_ready"), sem_("hot_ready"), sem_("turned"), sem_("copied"), sem_("looked_up"),
        sem_("z_step"), sem_("exp_ready"), sem_("value_ready"), sem_("summed"), sem_("added"))
    sorted_c = b.sorted_d.rearrange("(c p q) o -> c p (q o)", p=P, q=EQ)
    N = SUM_SLOTS
    MOST = (MAX_CHUNKS + N) // N

    def chunk(view, c):
        return view[bass.ds(c, 1)].rearrange("o p q -> (o p) q")

    def leaky(dve, t, v):
        t.then(nc.vector.scalar_tensor_tensor(v, v, 0.2, v, ALU.mult, ALU.max))

    with nc.Block() as block:
        @block.sync
        def _(sp):
            sp.dma_start(tiles_i[0:1, :], b.chunk_tile_d.rearrange("q p -> (q p)").rearrange("(o k) -> o k", o=1)
                         ).then_inc(setup_in, 16)
            sp.dma_start(loops_i[0:1, :], b.loops_d[:, :]).then_inc(setup_in, 16)
            sp.wait_ge(setup_in, 32)
            rounds = sp.value_load(loops_i[0:1, 1:2], min_val=1, max_val=MOST)
            with sp.Fori(0, rounds) as i:
                for s in R:
                    sp.wait_ge(value_ready, i * N)
                    sp.dma_start(word[s], chunk(sorted_c, i * N + s)).then_inc(chunk_in[s], 16)
                    sp.dma_start(got[s].rearrange("p q f -> p (q f)"), chunk(b.gathered_d, i * N + s)).then_inc(
                        chunk_in[s], 16)
            for s in R:
                sp.wait_ge(chunk_in[s], rounds * 32)
                sp.sem_inc(b.settled[2], 1)

        @block.vector
        def _(dve):
            t = Tally(dve, info_step)
            t.then(nc.vector.tensor_copy(info[:, :, 0:HEADS], table[:, :, HEADS + GAT:]))
            t.then(nc.vector.tensor_tensor(raw, top, info[:, :, 0:HEADS], ALU.add))
            leaky(dve, t, raw)
            t.then(nc.vector.tensor_copy(info[:, :, HEADS:], raw))
            nc.vector.memset(sums, 0.0).then_inc(added, 1)
            dve.wait_ge(setup_in, 32)
            rounds = dve.value_load(loops_i[0:1, 1:2], min_val=1, max_val=MOST)
            with dve.Fori(0, rounds) as i:
                first = i * N
                for s in R:
                    dve.wait_ge(chunk_in[s], (i + 1) * 32)
                    nc.vector.tensor_scalar(low[s], word[s], 255, None, ALU.bitwise_and).then_inc(low_ready, 1)
                for s in R:
                    dve.wait_ge(low_ready, first + (s + 1))
                    dve.wait_ge(summed, first)
                    nc.vector.tensor_tensor(hot[s], b.iota.unsqueeze(1).broadcast_to([P, EQ, P]),
                                            low[s].unsqueeze(2).broadcast_to([P, EQ, P]),
                                            ALU.is_equal).then_inc(hot_ready, 1)
                for s in R:
                    dve.wait_ge(looked_up, first + (s + 1))
                    t = Tally(dve, z_step, base=(first + s) * 3)
                    e = psum[:, 4 + s, 0:32].rearrange("p (q f) -> p q f", q=EQ)
                    t.then(nc.vector.tensor_tensor(z[s], got[s][:, :, 0:HEADS], e[:, :, 0:HEADS], ALU.add))
                    leaky(dve, t, z[s])
                    t.mark(nc.vector.tensor_tensor(z[s], z[s], e[:, :, HEADS:], ALU.subtract))
                for s in R:
                    dve.wait_ge(exp_ready, first + (s + 1))
                    nc.vector.tensor_tensor(
                        value[s][:, :, HEADS:].rearrange("p q (h e) -> p q h e", h=HEADS),
                        got[s][:, :, HEADS:HEADS + GAT].rearrange("p q (h e) -> p q h e", h=HEADS),
                        value[s][:, :, 0:HEADS].unsqueeze(3).broadcast_to([P, EQ, HEADS, EXPERTS]),
                        ALU.mult).then_inc(value_ready, 1)
                for s in R:
                    dve.wait_ge(summed, first + (s + 1))
                    dve.wait_ge(added, first + (s + 1))
                    tile = dve.value_load(tiles_i[0:1, bass.ds(first + s, 1)], min_val=0, max_val=TILES - 1)
                    a = sums[:, bass.ds(tile, 1), :].rearrange("p o f -> p (o f)")
                    nc.vector.tensor_tensor(a, a, psum[:, 4 + s, 32:32 + W], ALU.add).then_inc(added, 1)

        @block.tensor
        def _(pe):
            pe.wait_ge(info_step, 4)
            pe.wait_ge(setup_in, 32)
            rounds = pe.value_load(loops_i[0:1, 1:2], min_val=1, max_val=MOST)
            with pe.Fori(0, rounds) as i:
                first = i * N
                for s in R:
                    pe.wait_ge(hot_ready, first + (s + 1))
                    pe.wait_ge(copied, first)
                    for q in range(EQ):
                        last = nc.tensor.transpose(psum[:, s, q * P:(q + 1) * P], hot[s][:, q, :], b.ident)
                    last.then_inc(turned, 1)
                for s in R:
                    pe.wait_ge(copied, first + (s + 1))
                    pe.wait_ge(z_step, first * 3)
                    pe.wait_ge(added, first + 1)
                    tile = pe.value_load(tiles_i[0:1, bass.ds(first + s, 1)], min_val=0, max_val=TILES - 1)
                    for q in range(EQ):
                        last = nc.tensor.matmul(psum[:, 4 + s, 8 * q:8 * q + 8], hot_t[s][:, q, :],
                                                info[:, bass.ds(tile, 1), :].rearrange("p o f -> p (o f)"),
                                                start=True, stop=True)
                    last.then_inc(looked_up, 1)
                for s in R:
                    pe.wait_ge(value_ready, first + (s + 1))
                    for q in range(EQ):
                        last = nc.tensor.matmul(psum[:, 4 + s, 32:32 + W], hot[s][:, q, :], value[s][:, q, :],
                                                start=(q == 0), stop=(q == EQ - 1))
                    last.then_inc(summed, 1)

        @block.scalar
        def _(act):
            act.wait_ge(setup_in, 32)
            rounds = act.value_load(loops_i[0:1, 1:2], min_val=1, max_val=MOST)
            with act.Fori(0, rounds) as i:
                first = i * N
                for s in R:
                    act.wait_ge(turned, first + (s + 1))
                    act.wait_ge(looked_up, first)
                    nc.scalar.activation(hot_t[s].rearrange("p q e -> p (q e)"), psum[:, s, :], ACT.Copy).then_inc(
                        copied, 1)
                for s in R:
                    act.wait_ge(z_step, (first + (s + 1)) * 3)
                    act.wait_ge(summed, first)
                    nc.scalar.activation(value[s][:, :, 0:HEADS], z[s], ACT.Exp).then_inc(exp_ready, 1)


def route(nc, b):
    sem, carve, psum = b.sem, b.carve, b.psum
    W = HEADS + GAT
    table = carve(0, [TILES, TAB])
    at = TILES * (TAB + HEADS)
    sums = carve(at, [TILES, W])
    info = carve(at + TILES * W, [TILES, 2 * HEADS])
    at += TILES * (W + 2 * HEADS)
    own = carve(at, [TILES, HEADS])
    own_w = carve(at + 512, [TILES, HEADS])
    inv = carve(at + 1024, [TILES, HEADS])
    agg = carve(at + 1536, [TILES, GAT])
    wide = carve(at + 3584, [TILES, GAT])
    mean = carve(at + 5632, [TILES])
    var = carve(at + 5760, [TILES])
    std = carve(at + 5888, [TILES])
    rstd = carve(at + 6016, [TILES])
    tmp = carve(at + 6144, [TILES])
    score = carve(at + 6272, [TILES, EXPERTS])
    place = carve(at + 6784, [TILES, EXPERTS])
    beats = carve(at + 7296, [TILES])
    most = carve(at + 7424, [TILES])
    gates = b.xnt[:, 0, 0:TILES * EXPERTS].rearrange("p (t e) -> p t e", e=EXPERTS)
    step, own_ready, own_exp, var_ready, std_ready, less_ready, gate_exp = (
        sem("route_step"), sem("own_ready"), sem("own_exp"), sem("route_var_ready"), sem("route_std_ready"),
        sem("less_ready"), sem("gate_exp"))

    def per_token(v, n):
        return v.unsqueeze(2).broadcast_to([P, TILES, n])

    def per_column(v):
        return v.unsqueeze(1).broadcast_to([P, TILES, GAT])

    def by_head(v):
        return v.rearrange("p t (h e) -> p t h e", h=HEADS)

    with nc.Block() as block:
        @block.vector
        def _(dve):
            t = Tally(dve, step)
            v = nc.vector
            t.then(v.tensor_tensor(own, table[:, :, 0:HEADS], info[:, :, 0:HEADS], ALU.add))
            t.then(v.scalar_tensor_tensor(own, own, 0.2, own, ALU.mult, ALU.max))
            v.tensor_tensor(own, own, info[:, :, HEADS:], ALU.subtract).then_inc(own_ready, 1)
            dve.wait_ge(own_exp, 1)
            t.then(v.tensor_tensor(inv, sums[:, :, 0:HEADS], own_w, ALU.add))
            t.then(v.tensor_scalar(inv, inv, 1e-16, None, ALU.add))
            t.then(v.reciprocal(inv, inv))
            t.then(v.tensor_tensor(by_head(agg), by_head(table[:, :, HEADS:HEADS + GAT]),
                                   own_w.unsqueeze(3).broadcast_to([P, TILES, HEADS, EXPERTS]), ALU.mult))
            t.then(v.tensor_tensor(agg, agg, sums[:, :, HEADS:], ALU.add))
            t.then(v.tensor_tensor(by_head(agg), by_head(agg),
                                   inv.unsqueeze(3).broadcast_to([P, TILES, HEADS, EXPERTS]), ALU.mult))
            t.then(v.tensor_tensor(agg, agg, per_column(b.gat[:, 2, :]), ALU.add))
            t.then(v.tensor_reduce(mean, agg, AX.X, ALU.add))
            t.then(v.tensor_scalar(mean, mean, 1.0 / GAT, None, ALU.mult))
            t.then(v.tensor_tensor(agg, agg, per_token(mean, GAT), ALU.subtract))
            t.then(v.tensor_tensor(wide, agg, agg, ALU.mult))
            t.then(v.tensor_reduce(var, wide, AX.X, ALU.add))
            v.tensor_scalar(var, var, 1.0 / GAT, LN_G_EPS, ALU.mult, ALU.add).then_inc(var_ready, 1)
            dve.wait_ge(std_ready, 1)
            newton(nc, t, rstd, tmp, var, std)
            t.then(v.tensor_tensor(agg, agg, per_token(rstd, GAT), ALU.mult))
            t.then(v.tensor_tensor(agg, agg, per_column(b.gat[:, 3, :]), ALU.mult))
            t.then(v.tensor_tensor(agg, agg, per_column(b.gat[:, 4, :]), ALU.add))
            t.then(v.tensor_reduce(score, agg.rearrange("p t (h e) -> p t e h", h=HEADS), AX.X, ALU.add))
            t.then(v.tensor_scalar(score, score, 1.0 / HEADS, None, ALU.mult))
            t.then(v.memset(place, 0.0))
            for e in range(EXPERTS):
                for f in range(e + 1, EXPERTS):
                    t.then(v.tensor_tensor(beats, score[:, :, e], score[:, :, f], ALU.is_ge))
                    t.then(v.tensor_tensor(place[:, :, f], place[:, :, f], beats, ALU.add))
                    t.then(v.tensor_scalar(beats, beats, -1.0, 1.0, ALU.mult, ALU.add))
                    t.then(v.tensor_tensor(place[:, :, e], place[:, :, e], beats, ALU.add))
            t.then(v.tensor_reduce(most, score, AX.X, ALU.max))
            v.tensor_tensor(score, score, per_token(most, EXPERTS), ALU.subtract).then_inc(less_ready, 1)
            t.then(v.tensor_scalar(place, place, 2.0, None, ALU.is_lt))
            dve.wait_ge(gate_exp, 1)
            t.then(v.tensor_tensor(gates, gates, place, ALU.mult))
            t.then(v.tensor_reduce(most, gates, AX.X, ALU.add))
            t.then(v.reciprocal(most, most))
            t.then(v.tensor_tensor(gates, gates, per_token(most, EXPERTS), ALU.mult))

        @block.scalar
        def _(act):
            act.wait_ge(own_ready, 1)
            nc.scalar.activation(own_w, own, ACT.Exp).then_inc(own_exp, 1)
            act.wait_ge(var_ready, 1)
            nc.scalar.activation(std, var, ACT.Sqrt).then_inc(std_ready, 1)
            act.wait_ge(less_ready, 1)
            nc.scalar.activation(gates, score, ACT.Exp).then_inc(gate_exp, 1)


def combine(nc, b):
    sem, carve = b.sem, b.carve
    Q, SLOTS = 2, 3
    gates = b.xnt[:, 0, 0:TILES * EXPERTS].rearrange("p (t e) -> p t e", e=EXPERTS)
    y = [carve(s * Q * EXPERTS * D, [Q, EXPERTS, D]) for s in range(SLOTS)]
    acc = [carve(SLOTS * Q * EXPERTS * D + s * Q * D, [Q, D]) for s in range(SLOTS)]
    y_in, out_done = [sem(f"y_in{s}") for s in range(SLOTS)], [sem(f"out_done{s}") for s in range(SLOTS)]
    gated = sem("gated")
    y_q = b.y_d.rearrange("(n q) p (e d) -> n p q e d", q=Q, e=EXPERTS)
    x_q = b.x2_d.rearrange("(n q) p d -> n p q d", q=Q)
    out_q = b.out_t.rearrange("(n q) p d -> n p q d", q=Q)
    ROUNDS = TILES // Q
    LOOPS = ROUNDS // SLOTS

    with nc.Block() as block:
        @block.sync
        def _(sp):
            def load(n, s, before):
                if before is not None:
                    sp.wait_ge(out_done[s], before)
                sp.dma_start(y[s], y_q[bass.ds(n, 1)].rearrange("o p q e d -> (o p) q e d")).then_inc(y_in[s], 16)
                sp.dma_start(acc[s], x_q[bass.ds(n, 1)].rearrange("o p q d -> (o p) q d")).then_inc(y_in[s], 16)

            for s in range(SLOTS):
                load(s, s, None)
            with sp.Fori(1, LOOPS) as i:
                for s in range(SLOTS):
                    load(i * SLOTS + s, s, i * 16)
            for s in range(ROUNDS % SLOTS):
                load(LOOPS * SLOTS + s, s, LOOPS * 16)
            for s in range(SLOTS):
                sp.wait_ge(out_done[s], 16 * (LOOPS + (s < ROUNDS % SLOTS)))

        @block.vector
        def _(dve):
            def gate(n, s, round_):
                dve.wait_ge(y_in[s], (round_ + 1) * 32)
                for e in range(EXPERTS):
                    for q in range(Q):
                        k = n * Q + q
                        last = nc.vector.scalar_tensor_tensor(
                            acc[s][:, q, :], y[s][:, q, e, :],
                            gates[:, bass.ds(k, 1), e:e + 1].rearrange("p o k -> p (o k)"), acc[s][:, q, :],
                            ALU.mult, ALU.add)
                    last.then_inc(gated, 1)
                    dve.wait_ge(gated, n * EXPERTS + (e + 1))

            with dve.Fori(0, LOOPS) as i:
                for s in range(SLOTS):
                    gate(i * SLOTS + s, s, i)
            for s in range(ROUNDS % SLOTS):
                gate(LOOPS * SLOTS + s, s, LOOPS)

        @block.scalar
        def _(act):
            def store(n, s):
                act.wait_ge(gated, (n + 1) * EXPERTS)
                act.dma_start(out_q[bass.ds(n, 1)].rearrange("o p q d -> (o p) q d"), acc[s]).then_inc(
                    out_done[s], 16)

            with act.Fori(0, LOOPS) as i:
                for s in range(SLOTS):
                    store(i * SLOTS + s, s)
            for s in range(ROUNDS % SLOTS):
                store(LOOPS * SLOTS + s, s)


_ORDER = ["x", "L0_ffn_W_gat", "L0_ffn_att_src", "L0_ffn_att_dst", "L0_ffn_b_gat", "L0_ffn_ln_gamma",
          "L0_ffn_ln_beta", "L0_ffn_W1", "L0_ffn_b1", "L0_ffn_W2", "L0_ffn_b2", "L0_ffn_edge_index"]


def program(nc, inputs):
    arrays, args = {}, []
    for name in _ORDER:
        a = np.ascontiguousarray(inputs[name])
        arrays[f"in_{name}"] = a
        args.append(nc.dram_tensor(f"in_{name}", a.shape, mybir.dt.from_np(a.dtype), kind="ExternalInput").ap())
    c = shape_constants()
    arrays["in_constants"] = c
    args.append(nc.dram_tensor("in_constants", c.shape, F32, kind="ExternalInput").ap())
    args.append(nc.dram_tensor("out_0", (IMAGES, SIDE, SIDE, D), F32, kind="ExternalOutput").ap())
    build(nc, *args)
    return arrays


def kernel(**inputs):
    import concourse.bacc as bacc
    from concourse.bass_utils import run_bass_kernel_spmd
    nc = bacc.Bacc("TRN2", target_bir_lowering=False, num_devices=1)
    arrays = program(nc, inputs)
    r = run_bass_kernel_spmd(nc, [arrays], core_ids=[0])
    return r.results[0]["out_0"]
```
